# Optimizing a Trainium2 kernel written in Bass

```python
import numpy as np
import jax
import jax.numpy as jnp

def _softmax(x, axis=-1):
    return jax.nn.softmax(x, axis=axis)

def _gelu(x):
    return jax.nn.gelu(x, approximate=True)

def _silu(x):
    return jax.nn.silu(x)

def _sigmoid(x):
    return jax.nn.sigmoid(x)

def _layernorm(x, axis=-1, eps=1e-05):
    m = jnp.mean(x, axis=axis, keepdims=True)
    v = jnp.var(x, axis=axis, keepdims=True)
    return (x - m) / jnp.sqrt(v + eps)

def _scatter_add(tgt, idx, src, axis=0):
    return tgt.at[idx].add(src)

def _segment_sum(src, seg, n):
    return jax.ops.segment_sum(src, seg, n)
kernel_name = 'mk_adj_resnorm_d2_adj_r2_7cbf16'

def setup_inputs(seed: int=0):
    np.random.seed(seed)
    _w = jnp.asarray

    def _rec_inputs():
        import jax
        import jax.numpy as jnp
        _gk = jax.random.key(seed)
        x = -0.0005207 + 1.001 * jax.random.normal(jax.random.fold_in(_gk, 1), (8192, 128), jnp.float32)
        _a = jax.random.bernoulli(jax.random.fold_in(_gk, 2), 0.000976562, (8192, 8192))
        _a = jnp.logical_or(_a, jnp.swapaxes(_a, -1, -2))
        _a = jnp.logical_or(_a, jnp.eye(8192, dtype=bool))
        adj = _a.astype(jnp.int32)
        return (x, adj)
    x, adj = _rec_inputs()

    def _L0_gnn_setup():
        import jax, jax.numpy as jnp
        import numpy as np
        N = 4096
        IN_F = 128
        OUT_F = 128
        key = jax.random.key(seed)
        k_v, k_adj, k1, k2, k3, kb = jax.random.split(key, 6)
        stdv = 1.0 / np.sqrt(OUT_F)
        V = jax.random.normal(k_v, (N, IN_F), dtype=jnp.float32)
        adj = jax.random.randint(k_adj, (N, N), 0, 4, dtype=jnp.int32)
        w1 = jax.random.uniform(k1, (IN_F, OUT_F), jnp.float32, -stdv, stdv)
        w2 = jax.random.uniform(k2, (IN_F, OUT_F), jnp.float32, -stdv, stdv)
        w3 = jax.random.uniform(k3, (IN_F, OUT_F), jnp.float32, -stdv, stdv)
        bias = jax.random.uniform(kb, (OUT_F,), jnp.float32, -stdv, stdv)
        return {'V': V, 'adj': adj, 'w1': w1, 'w2': w2, 'w3': w3, 'bias': bias}
    _L0_gnn_all = _L0_gnn_setup()
    _L0_gnn_in = {k: v for k, v in _L0_gnn_all.items() if k in ('w1', 'w2', 'w3', 'bias')}
    del _L0_gnn_all

    def _L1_gnn_setup():
        import jax, jax.numpy as jnp
        import numpy as np
        NEG_INF = -9000000000000000.0
        LEAKY_SLOPE = 0.01
        key = jax.random.key(seed)
        ks = jax.random.split(key, 8)
        N, D = (4096, 128)
        X = jax.random.normal(ks[0], (N, D), dtype=jnp.float32)
        adj = jax.random.randint(ks[1], (N, N), 0, 2, dtype=jnp.int32)
        W = jax.random.normal(ks[2], (D, D), dtype=jnp.float32) * (1.0 / np.sqrt(D))
        b = jax.random.normal(ks[3], (D,), dtype=jnp.float32) * 0.01
        we1 = jax.random.normal(ks[4], (D, 1), dtype=jnp.float32) * (1.0 / np.sqrt(D))
        be1 = jax.random.normal(ks[5], (1,), dtype=jnp.float32) * 0.01
        we2 = jax.random.normal(ks[6], (D, 1), dtype=jnp.float32) * (1.0 / np.sqrt(D))
        be2 = jax.random.normal(ks[7], (1,), dtype=jnp.float32) * 0.01
        return {'X': X, 'adj': adj, 'W': W, 'b': b, 'we1': we1, 'be1': be1, 'we2': we2, 'be2': be2}
    _L1_gnn_all = _L1_gnn_setup()
    _L1_gnn_in = {k: v for k, v in _L1_gnn_all.items() if k in ('W', 'b', 'we1', 'be1', 'we2', 'be2')}
    del _L1_gnn_all
    return {'x': x, 'adj': adj, 'L0_gnn_w1': _L0_gnn_in['w1'], 'L0_gnn_w2': _L0_gnn_in['w2'], 'L0_gnn_w3': _L0_gnn_in['w3'], 'L0_gnn_bias': _L0_gnn_in['bias'], 'L1_gnn_W': _L1_gnn_in['W'], 'L1_gnn_b': _L1_gnn_in['b'], 'L1_gnn_we1': _L1_gnn_in['we1'], 'L1_gnn_be1': _L1_gnn_in['be1'], 'L1_gnn_we2': _L1_gnn_in['we2'], 'L1_gnn_be2': _L1_gnn_in['be2']}

def reference(x, adj, L0_gnn_w1, L0_gnn_w2, L0_gnn_w3, L0_gnn_bias, L1_gnn_W, L1_gnn_b, L1_gnn_we1, L1_gnn_be1, L1_gnn_we2, L1_gnn_be2):
    import jax
    import jax.numpy as jnp

    def _L0_gnn_ref(V, adj, w1, w2, w3, bias):
        import jax, jax.numpy as jnp
        import numpy as np
        N = 4096
        IN_F = 128
        OUT_F = 128
        o1 = jnp.matmul((adj == 1).astype(jnp.float32), jnp.matmul(V, w1))
        o2 = jnp.matmul((adj == 2).astype(jnp.float32), jnp.matmul(V, w2))
        o3 = jnp.matmul((adj == 3).astype(jnp.float32), jnp.matmul(V, w3))
        return o1 + o2 + o3 + bias

    def _L1_gnn_ref(X, adj, W, b, we1, be1, we2, be2):
        import jax, jax.numpy as jnp
        import numpy as np
        NEG_INF = -9000000000000000.0
        LEAKY_SLOPE = 0.01
        h = X @ W.T + b
        e1 = h @ we1 + be1
        e2 = h @ we2 + be2
        e = e1 + e2.T
        e = jnp.where(e >= 0, e, LEAKY_SLOPE * e)
        scores = jnp.where(adj > 0, e, NEG_INF)
        attention = jax.nn.softmax(scores, axis=1)
        return attention @ h
    x = _layernorm(x + _L0_gnn_ref(x, adj, L0_gnn_w1, L0_gnn_w2, L0_gnn_w3, L0_gnn_bias), axis=-1)
    x = _layernorm(x + _L1_gnn_ref(x, adj, L1_gnn_W, L1_gnn_b, L1_gnn_we1, L1_gnn_be1, L1_gnn_we2, L1_gnn_be2), axis=-1)
    return x

_drawn_inputs = setup_inputs


def setup_inputs(seed=0):
    import zlib

    import numpy as np

    out = dict(_drawn_inputs(seed))
    spreads = {}
    factors = {'L1_gnn_b': 6.752}
    for name, (base, spread) in spreads.items():
        noise = np.random.default_rng([zlib.crc32(name.encode()), seed]).standard_normal(out[name].shape)
        drawn = base * np.exp(spread * noise) if base else spread * noise
        out[name] = jnp.asarray(drawn.astype(out[name].dtype))
    for name, factor in factors.items():
        out[name] = (out[name] * factor).astype(out[name].dtype)
    return out
```

```python
from contextlib import ExitStack

import concourse.bass as bass
from concourse import mybir

F32, BF16, F16 = mybir.dt.float32, mybir.dt.bfloat16, mybir.dt.float16
U16, I32 = mybir.dt.uint16, mybir.dt.int32
ALU = mybir.AluOpType
ACT = mybir.ActivationFunctionType
AX = mybir.AxisListType.X
ds = bass.ds

P = 128
D = 128
GT = 4
GR = GT * P
CB = 4
CC = CB * P
NBUF = 4
LO = 2048.0
BSC = 1024.0
SLOPE = 0.01
EPS = 1e-5
STEEP = 1e20
TB = D + 1
SPAN = 16.0
H_MAX = 60.0
NO_EDGE = -9e15
VB = 2 * CB


def build(nc, x, adj, w1, w2, w3, bias, W, b, we1, be1, we2, be2, out):
    N = x.shape[0]
    G = N // GR
    JB = N // P
    NC = N // CC
    NP = 2 * NC
    NQ = 2 * JB // VB
    W_ALL = 16 * 11
    PAIRS = NC // 2

    with ExitStack() as ctx:
        def sb(name, shape, dt):
            return ctx.enter_context(nc.sbuf_tensor(name, shape, dt))

        def sem(name):
            return ctx.enter_context(nc.semaphore(name))

        x1_dram = nc.dram_tensor("x1_scratch", (N, D), F32).ap()
        e1_dram = nc.dram_tensor("e1_scratch", (G, P, GT), F32).ap()
        e2_dram = nc.dram_tensor("e2_scratch", (JB, P), F32).ap()

        edges = sb("edges", [P, JB, GR], U16)
        h_sb = sb("h_sb", [P, JB, D], F32)
        x_in = h_sb
        tab = sb("tab", [P, 2, JB, 2 * TB], F16)
        tab_flat = tab[:, :, :, :].rearrange("p a j c -> p (a j c)")
        o_v, o_a = 0, JB * 2 * D
        o_t = o_a + NBUF * GT * CC
        o_m = o_t + 4 * 2 * GR
        assert o_m + GT * CC <= 2 * JB * 2 * TB or N < 8192
        if N < 8192:
            tab_flat = sb("pass_area", [P, o_m + GT * CC], F16)[:, :]
        v_hl = tab_flat[:, o_v:o_a].rearrange("p (j c) -> p j c", c=2 * D)
        adj_sb = tab_flat[:, o_a:o_t].bitcast(BF16).rearrange("p (n t c) -> p n t c", n=NBUF, t=GT)
        adjT = tab_flat[:, o_t:o_m].bitcast(BF16).rearrange("p (n c) -> p n c", n=4)
        largest = tab_flat[:, o_m:o_m + GT * CC].bitcast(BF16)
        work = sb("work", [P, 6 * CC * CB // 2], F32)
        masks = work[:, :].bitcast(BF16).rearrange("p (k n c) -> p k n c", k=3, n=2)
        gate, pos, neg = masks[:, 0], masks[:, 1], masks[:, 2]
        epi = [work[:, GR * n:GR * (n + 1)].rearrange("p (t c) -> p t c", t=GT) for n in range(6)]
        xg, y_tmp, yT_sb, v_sb, x1_sb, x1T_sb = epi[:6]
        stage = sb("stage", [P, 2, VB, D], F32)
        e1_row = sb("e1_row", [P, 2, GR], F32)
        hf = h_sb[:, :, :].rearrange("p j c -> p (j c)")
        if N < 8192:
            hf = sb("epi1", [P, 5 * GT * TB + 3 * GR + CC * CB], F32)[:, :]
        o_n = 4 * GT * TB
        o_x = o_n + GT * TB
        pos_part, neg_part = [hf[:, n * GT * 2 * TB:(n + 1) * GT * 2 * TB]
                              .rearrange("p (t c) -> p t c", t=GT) for n in range(2)]
        num_den = hf[:, o_n:o_n + GT * TB].rearrange("p (t c) -> p t c", t=GT)
        x1_in, v2, out_sb = [hf[:, o_x + GR * n:o_x + GR * (n + 1)].rearrange("p (t c) -> p t c", t=GT)
                             for n in range(3)]
        tab_f32 = tab[:, :, :, :].rearrange("p a j c -> p (a j c)").bitcast(F32)
        score, e2_row = tab_f32[:, 0:N], tab_f32[:, N:2 * N]
        adj_row = edges[:, :, :].rearrange("p j r -> p (j r)").bitcast(BF16)[:, 0:N]
        prob_T = work[:, 0:CC].rearrange("p (t c) -> p t c", t=CB)
        x1_tile, v_tile, out_tile = [work[:, CC + n * D:CC + (n + 1) * D] for n in range(3)]
        e2_T = work[0:JB, CC + 3 * D:CC + 3 * D + P]
        tile_col = work[:, CC + 4 * D:CC + 4 * D + 8]
        o_b = o_x + 3 * GR
        bit_buf = hf[:, o_b:o_b + CC * CB].bitcast(U16).rearrange("p (n c) -> p n c", n=2)
        w_sb = [sb(f"w{n}_sb", [P, D], F32)[:, :] for n in (1, 2, 3)]
        W_sb, WT, idf, onesq, hsum = [sb(n, [P, D], F32)[:, :] for n in ("W_sb", "WT", "idf", "onesq", "hsum")]
        idb = sb("idb", [P, P], BF16)
        biases = sb("biases", [P, 2 * D + 2], F32)
        c12 = sb("c12", [P, 2], F32)
        b_sq = sb("b_sq", [P, P], F32)
        b_col = sb("b_col", [P, 1], F32)
        we = sb("we", [P, 2], F32)
        u12 = sb("u12", [P, 2], F32)
        pow2 = sb("pow2", [P, 3, 16], F32)
        scale = sb("scale", [P, 1], F32)
        bits = sb("bits", [P, 16], U16)
        stats = sb("stats", [P, GT, 6], F32)
        mv = sb("mv", [P, GT, 2], F32)
        var = sb("var", [P, GT], F32)
        sd = sb("sd", [P, GT], F32)
        rs = sb("rs", [P, GT], F32)
        zr = sb("zr", [P, GT], F32)
        dn = sb("dn", [P, GT], F32)
        rd = sb("rd", [P, GT], F32)
        e12 = sb("e12", [P, 2, JB], F32)
        cols = sb("cols", [P, 10, JB], F32)
        (e2s, tt, lt, mx, ta, tc, a_row, c_row, bb, dd) = [cols[:, n, :] for n in range(10)]
        top = sb("top", [P, 4], F32)
        tops = sb("tops", [P, 4], F32)
        flag = sb("flag", [P, 2], I32)
        wide = sb("wide", [P, 4], F32)
        ne = sb("ne", [P, 2], F32)

        ps = ctx.enter_context(nc.psum_tensor("ps", [P, 8, GR], F32))
        E0, E1 = ps[:, 6, :], ps[:, 7, :]
        E0t, E1t = [e.rearrange("p (t c) -> p t c", t=GT) for e in (E0, E1)]
        y_high, y_low = ps[:, 4, :], ps[:, 5, :]
        y_high_t, y_low_t = [y.rearrange("p (t c) -> p t c", t=GT) for y in (y_high, y_low)]

        h_all = ps[:, 7, 3 * P:4 * P]
        factor = (mx, tt)

        def turned(n):
            return ps[:, 2 * n:2 * n + 2, :]

        def sems(*names):
            return [sem(n) for n in names]

        s_x, s_w, s_ident, s_const = sems("x_in", "weights_in", "identities", "constants")
        s_bsq, s_setup, s_setc = sems("b_spread", "setup_products", "setup_copied")
        s_vh, s_vr, s_vl = sems("x_high", "x_rest", "x_low")
        s_adj = [sem(f"adj_in_{n}") for n in range(NBUF)]
        s_turn, s_evac, s_mul, s_chk, s_pack = sems("adj_turned", "adjT_ready", "multiplied", "checked", "packed")
        names = ("y_half", "y_ready", "o_ready", "xg_in", "v_ready", "stats_ready",
                 "mean_ready", "var_ready", "sd_ready", "rs_ready", "x1_ready", "x1_turned", "x1T_ready",
                 "h_ready", "xb_ready", "e_ready", "e_copied", "x1_stored", "e1_stored", "scale_ready")
        fast = {name: sem(name) for name in names}
        general = {name: sem("general_" + name) for name in names}
        g_in, g_mask, g_turn, g_evac, g_mul, g_pack, g_zero = sems(
            "general_adj_in", "general_masked", "general_turned", "general_adjT_ready",
            "general_multiplied", "general_packed", "general_zeroed")
        wide_names = ("e2_turned", "e2_copied", "e2_stored", "e2_row_in", "adj_in", "penalty", "score", "leaky",
                      "masked", "max", "max_negated", "exp", "sum", "turned", "copied", "product", "x1_in", "v",
                      "stats", "mean", "var", "sd", "scale", "out", "stored")
        wd = {name: sem("wide_" + name) for name in wide_names}
        s_top, s_all, s_flag, s_wide, s_hbound, s_minus, s_span, s_exps, s_exp, s_mid = sems(
            "tops", "tops_of_all", "flag_ready", "wide_flag_ready", "h_bound", "minus_e2", "span", "exponents",
            "exponentials", "mid_chain")
        s_factor, s_full, s_high, s_low, s_hs, s_hsc = sems(
            "factors_ready", "table_full", "table_high", "table_low", "hsum_ready", "hsum_copied")
        s_row = [sem(f"e1_row_in_{n}") for n in range(2)]
        s_gate, s_bit, s_pos, s_neg, s_used = sems(
            "gates_ready", "edge_bits_ready", "pos_ready", "neg_ready", "masks_used")
        s_acc, s_ppart, s_npart, s_add, s_x1in, s_v2, s_var2, s_sd2, s_out, s_stored = sems(
            "sums_done", "pos_parts_ready", "neg_parts_ready", "parts_added", "x1_in",
            "v2_ready", "var2_ready", "sd2_ready", "out_ready", "out_stored")
        s_num, s_zr, s_dn, s_rd, s_st2, s_mv2, s_rs2 = sems(
            "numerators_ready", "empty_rows", "denominators_ready", "reciprocals_ready", "stats2_ready",
            "mean2_ready", "rs2_ready")

        def ge(eng, s, value):
            if not (isinstance(value, int) and value <= 0):
                eng.wait_ge(s, value)

        def some(eng, lo, hi, body):
            if hi > lo:
                with eng.Fori(lo, hi) as i:
                    body(i)

        def in_twos(eng, end, body):
            assert end % 2 == 0

            def both(i):
                body(2 * i + 1, 1)
                body(2 * i + 2, 0)

            some(eng, 0, end // 2 - 1, both)
            body(end - 1, 1, last=True)

        def spot(k):
            return k * NC // 16


        def dve_y(e, S, n, g):
            e.tensor_scalar(y_tmp, y_low_t, pow2[:, 2, ds(g, 1)], None, ALU.mult).then_inc(S["y_half"], 1)
            e.wait_ge(S["y_half"], n + 1)
            e.scalar_tensor_tensor(yT_sb, y_high_t, pow2[:, 1, ds(g, 1)], y_tmp,
                                   ALU.mult, ALU.add).then_inc(S["y_ready"], 1)

        def pe_o(e, S, n, w, first_product):
            e.wait_ge(S["y_ready"], n + 1)
            if not first_product:
                e.wait_ge(S["v_ready"], n)
            for t in range(GT):
                last = e.matmul(E1t[:, t, :], yT_sb[:, t, :], w[:, :], start=True, stop=True)
            last.then_inc(S["o_ready"], 1)

        def sp_xg(e, S, g):
            e.dma_start(xg, x[ds(g * GR, GR), :].rearrange("(t p) f -> p t f", p=P)).then_inc(S["xg_in"], 16)

        def pool_xb(e, S, g):
            e.wait_ge(S["xg_in"], 16 * (g + 1))
            e.tensor_tensor(xg, xg, biases[:, 0:D].unsqueeze(1).broadcast_to([P, GT, D]), ALU.add)\
                .then_inc(S["xb_ready"], 1)

        def dve_v(e, S, n, g, first_product, last_product):
            e.wait_ge(S["o_ready"], n + 1)
            if first_product:
                e.wait_ge(S["xb_ready"], g + 1)
            else:
                e.wait_ge(S["v_ready"], n)
            e.tensor_tensor(v_sb, E1t, xg if first_product else v_sb, ALU.add).then_inc(S["v_ready"], 1)
            if last_product:
                e.wait_ge(S["v_ready"], n + 1)
                for t in range(GT):
                    last = e.bn_stats(stats[:, t, :], v_sb[:, t, :])
                last.then_inc(S["stats_ready"], 1)
                e.wait_ge(S["stats_ready"], g + 1)
                e.memset(var[:, :], 0.0)
                for t in range(GT):
                    last = e.bn_aggr(mv[:, t, :], stats[:, t, :])
                last.then_inc(S["mean_ready"], 1)
                e.wait_ge(S["mean_ready"], g + 1)
                e.tensor_scalar(var[:, :], mv[:, :, 1], EPS, None, ALU.add).then_inc(S["var_ready"], 1)

        def act_sd(e, S, g):
            e.wait_ge(S["var_ready"], g + 1)
            e.activation(sd[:, :], var[:, :], ACT.Sqrt).then_inc(S["sd_ready"], 1)

        def dve_x1(e, S, g):
            e.wait_ge(S["sd_ready"], g + 1)
            e.reciprocal(rs[:, :], sd[:, :]).then_inc(S["rs_ready"], 1)
            e.wait_ge(S["rs_ready"], g + 1)
            for t in range(GT):
                last = e.tensor_scalar(x1_sb[:, t, :], v_sb[:, t, :], mv[:, t, 0:1], rs[:, t:t + 1],
                                       ALU.subtract, ALU.mult)
            last.then_inc(S["x1_ready"], 1)

        def sp_x1(e, S, g):
            e.wait_ge(S["x1_ready"], g + 1)
            e.dma_start(x1_dram[ds(g * GR, GR), :].rearrange("(t p) f -> p t f", p=P), x1_sb)\
                .then_inc(S["x1_stored"], 16)
            e.wait_ge(S["x1_stored"], 16 * (g + 1))

        def sp_e1(e, S, g):
            e.wait_ge(S["e_copied"], g + 1)
            e.dma_start(e1_dram[ds(g, 1)].rearrange("a p t -> p (a t)"), e12[:, 0, ds(g * GT, GT)])\
                .then_inc(S["e1_stored"], 16)

        def pe_x1T(e, S, g):
            e.wait_ge(S["x1_ready"], g + 1)
            for t in range(GT):
                last = e.transpose(E0t[:, t, :], x1_sb[:, t, :], idf[:, :])
            last.then_inc(S["x1_turned"], 1)

        def act_x1T(e, S, g):
            e.wait_ge(S["x1_turned"], g + 1)
            e.activation(x1T_sb, E0t, ACT.Copy).then_inc(S["x1T_ready"], 1)

        def pe_h(e, S, g):
            e.wait_ge(S["x1T_ready"], g + 1)
            for t in range(GT):
                last = e.matmul(E0t[:, t, :], x1T_sb[:, t, :], WT[:, :], start=True, stop=True)
            last.then_inc(S["h_ready"], 1)
            for t in range(GT):
                last = e.matmul(E1[:, 2 * t:2 * t + 2], x1T_sb[:, t, :], u12[:, :], start=True, stop=True)
            last.then_inc(S["e_ready"], 1)

        def dve_h(e, S, g):
            e.wait_ge(S["h_ready"], g + 1)
            e.tensor_tensor(h_sb[:, ds(g * GT, GT), :], E0t,
                            biases[:, D:2 * D].unsqueeze(1).broadcast_to([P, GT, D]), ALU.add)

        def dve_e(e, S, g):
            e.wait_ge(S["e_ready"], g + 1)
            e.tensor_tensor(e12[:, :, ds(g * GT, GT)], E1[:, 0:2 * GT].rearrange("p (t k) -> p k t", k=2),
                            c12[:, :].unsqueeze(2).broadcast_to([P, 2, GT]), ALU.add).then_inc(S["e_copied"], 1)

        def turn(e, buf, c, i):
            for jj in range(2):
                for t in range(GT):
                    j = 2 * i + jj
                    last = e.matmul(ps[:, 2 * c + jj, t * P:(t + 1) * P], adj_sb[:, buf, t, j * P:(j + 1) * P],
                                    idb[:, :], start=True, stop=True)
            return last

        def multiply(e, slot, j, first, final):
            for jj in range(2):
                for k, y in enumerate((y_high, y_low)):
                    last = e.matmul(y, v_hl[:, ds(j + jj, 1), k * D:(k + 1) * D].rearrange("p a c -> p (a c)"),
                                    adjT[:, slot, jj * GR:(jj + 1) * GR],
                                    start=first and jj == 0, stop=final and jj == 1)
            return last

        def sums_done(e, g, t):
            if t < GT - 1:
                e.wait_ge(s_acc, (GT - 1) * g + t + 1)
            else:
                e.wait_ge(s_used, NC * (g + 1))

        MASKS = [(ALU.is_equal, 1.0, w_sb[0]), (ALU.is_equal, 2.0, w_sb[1]), (ALU.is_equal, 3.0, w_sb[2]),
                 (ALU.is_gt, 0.0, None)]
        NM = len(MASKS)

        blk = ctx.enter_context(nc.Block())

        @blk.sync
        def _(e):
            xt = x.rearrange("(j p) f -> p j f", p=P)
            for v in range(JB // VB):
                ge(e, s_x, 16 * v)
                if v > 1:
                    e.wait_ge(s_adj[(v - 1) % NBUF], 16 * ((v - 1) // NBUF + 1))
                e.dma_start(x_in[:, v * VB:(v + 1) * VB, :], xt[:, v * VB:(v + 1) * VB, :]).then_inc(s_x, 16)
            row = lambda a: a.rearrange("(a n) -> a n", a=1).broadcast_to([P, a.shape[0]])
            loads = [(w_sb[0], w1), (w_sb[1], w2), (w_sb[2], w3), (W_sb, W), (biases[:, 0:D], row(bias)),
                     (biases[:, D:2 * D], row(b)), (biases[:, 2 * D:2 * D + 1], row(be1)),
                     (biases[:, 2 * D + 1:2 * D + 2], row(be2)),
                     (b_col[:, :], b.rearrange("(p a) -> p a", a=1)), (we[:, 0:1], we1), (we[:, 1:2], we2)]
            for dst, src in loads:
                e.dma_start(dst, src).then_inc(s_w, 16)
            assert 16 * len(loads) == W_ALL
            sp_xg(e, fast, 0)

            def turn_of(S, g):
                sp_x1(e, S, g)
                sp_xg(e, S, g + 1)
                sp_e1(e, S, g)

            some(e, 0, G - 1, lambda g: turn_of(fast, g))
            sp_x1(e, fast, G - 1)
            sp_e1(e, fast, G - 1)
            e.wait_ge(fast["e1_stored"], 16 * G)

            e.wait_ge(s_flag, 1)
            with e.If(e.value_load(flag[0:1, 0:1], min_val=0, max_val=1) > 0):
                sp_xg(e, general, 0)
                some(e, 0, G - 1, lambda g: turn_of(general, g))
                sp_x1(e, general, G - 1)
                sp_e1(e, general, G - 1)
                e.wait_ge(general["e1_stored"], 16 * G)
                e.wait_ge(s_wide, 2)

            def row_of(g, turn):
                ge(e, s_gate, NC * (g - 1))
                e.dma_start(e1_row[:, turn, :],
                            e1_dram[ds(g, 1)].rearrange("a p t -> a (p t)").broadcast_to([P, GR]))\
                    .then_inc(s_row[turn], 16)

            def x1_of(g):
                e.dma_start(x1_in, x1_dram[ds(g * GR, GR), :].rearrange("(t p) f -> p t f", p=P))\
                    .then_inc(s_x1in, 16)

            def store(g):
                e.wait_ge(s_out, g + 1)
                e.dma_start(out[ds(g * GR, GR), :].rearrange("(t p) f -> p t f", p=P), out_sb)\
                    .then_inc(s_stored, 16)

            row_of(0, 0)
            row_of(1, 1)
            e.wait_ge(s_wide, 1)
            with e.If(e.value_load(flag[0:1, 1:2], min_val=0, max_val=1) > 0):
                e.wait_ge(wd["e2_copied"], 1)
                e.dma_start(e2_dram, e2_T).then_inc(wd["e2_stored"], 16)
                e.wait_ge(wd["e2_stored"], 16)
                e.dma_start(e2_row, e2_dram.rearrange("(a j) p -> a (j p)", a=1).broadcast_to([P, N]))\
                    .then_inc(wd["e2_row_in"], 16)
                e.sem_inc(wd["stored"], 16)
                with e.Fori(0, JB) as i:
                    e.wait_ge(wd["stored"], 16 * (i + 1))
                    e.dma_start(x1_tile, x1_dram[ds(i * P, P), :]).then_inc(wd["x1_in"], 16)
                    e.wait_ge(wd["out"], i + 1)
                    e.dma_start(out[ds(i * P, P), :], out_tile).then_inc(wd["stored"], 16)
                e.wait_ge(wd["stored"], 16 * (JB + 1))
            with e.If(e.value_load(flag[0:1, 1:2], min_val=0, max_val=1) < 1):
                e.wait_ge(s_low, NQ)
                e.wait_ge(s_hsc, 1)
                x1_of(0)

                def turn_of1(g, turn, last=False):
                    if not last:
                        row_of(g + 1, 1 - turn)
                    store(g - 1)
                    e.wait_ge(s_stored, 16 * g)
                    x1_of(g)

                in_twos(e, G, turn_of1)
                store(G - 1)
                e.wait_ge(s_stored, 16 * G)

        @blk.gpsimd
        def _(e):
            def load(k, g, c):
                ge(e, s_turn, 2 * (k - NBUF + 1))
                ge(e, s_chk, k - NBUF + 2)
                e.dma_start(adj_sb[:, c % NBUF], adj[ds(g * GR, GR), c * CC:(c + 1) * CC]
                            .rearrange("(t p) c -> p t c", p=P)).then_inc(s_adj[c % NBUF], 16)

            for c in range(NBUF):
                load(c, 0, c)
            e.memset(idf[:, :], 0.0).then_inc(s_ident, 1)
            e.memset(idb[:, :], 0.0).then_inc(s_ident, 1)
            e.wait_ge(s_ident, 2)
            for m in (idb, idf):
                e.affine_select(out=m[:, :], in_=m[:, :], compare_op=ALU.not_equal, fill=1.0, base=0,
                                pattern=[[-1, P]], channel_multiplier=1).then_inc(s_ident, 1)
            for c in range(NBUF, NC):
                load(c, 0, c)

            e.wait_ge(s_w, W_ALL)

            def group(g):
                for c in range(NC):
                    load(g * NC + c, g, c)
                    if c == spot(2):
                        pool_xb(e, fast, g - 1)

            some(e, 1, G, group)
            pool_xb(e, fast, G - 1)

            def all_tops(n):
                e.wait_ge(s_top, n)
                e.partition_all_reduce(tops[:, :], top[:, :], P, bass.bass_isa.ReduceOp.max).then_inc(s_all, 1)

            all_tops(1)
            e.wait_ge(s_flag, 1)
            with e.If(e.value_load(flag[0:1, 0:1], min_val=0, max_val=1) > 0):
                with e.Fori(0, G) as g:
                    pool_xb(e, general, g)
                    for m in range(NM):
                        with e.Fori(0, NC) as c:
                            e.wait_ge(g_turn, 2 * ((g * NM + m) * NC + c) + 2)
                            e.dma_start(adj_sb[:, 0], adj[ds(g * GR, GR), ds(c * CC, CC)]
                                        .rearrange("(t p) c -> p t c", p=P)).then_inc(g_in, 16)

                all_tops(2)
                e.wait_ge(s_wide, 2)

            e.wait_ge(s_wide, 1)
            with e.If(e.value_load(flag[0:1, 1:2], min_val=0, max_val=1) > 0):
                with e.Fori(0, JB) as i:
                    e.wait_ge(wd["stored"], 16 * (i + 1))
                    e.dma_start(adj_row, adj[ds(i * P, P), :]).then_inc(wd["adj_in"], 16)
            with e.If(e.value_load(flag[0:1, 1:2], min_val=0, max_val=1) < 1):
                def full(q):
                    v, k = divmod(q, 2)
                    sl = slice(v * VB, (v + 1) * VB)
                    ge(e, s_low, q - 1)
                    e.tensor_tensor(stage[:, k], h_sb[:, sl, :],
                                    factor[k][:, sl].unsqueeze(2).broadcast_to([P, VB, D]),
                                    ALU.mult).then_inc(s_full, 1)

                for q in range(NQ):
                    if q < 2:
                        e.wait_ge(s_factor, q + 1)
                    full(q)

                def add(g):
                    e.wait_ge(s_ppart, GT * (g + 1))
                    e.wait_ge(s_npart, GT * (g + 1))
                    e.tensor_tensor(pos_part, pos_part, neg_part, ALU.add).then_inc(s_add, 1)

                some(e, 0, G, add)

        @blk.vector
        def _(e):
            e.memset(largest, 0.0).then_inc(s_chk, 1)
            e.memset(onesq[:, :], 1.0)
            for g in range(16):
                e.memset(pow2[:, 0, g:g + 1], 2.0 ** g)
                e.memset(pow2[:, 1, g:g + 1], 2.0 ** -g)
                e.memset(pow2[:, 2, g:g + 1], 2.0 ** -g / LO)
                last = e.memset(bits[:, g:g + 1], 1 << g)
            last.then_inc(s_const, 1)
            e.wait_ge(s_const, 1)

            def split_rest(v):
                e.wait_ge(s_vh, v + 1)
                sl = slice(v * VB, (v + 1) * VB)
                e.tensor_tensor(x_in[:, sl, :], x_in[:, sl, :], v_hl[:, sl, 0:D], ALU.subtract).then_inc(s_vr, 1)

            def pack(g, c):
                e.wait_ge(s_evac, 2 * (g * NC + c) + 2)
                dst = edges[:, CB * c:CB * (c + 1), :].rearrange("p j r -> p (j r)")
                two = 2 * (c % 2)
                src = adjT[:, two:two + 2, :].rearrange("p n c -> p (n c)")
                if isinstance(g, int) and g == 0:
                    e.tensor_copy(dst, src).then_inc(s_pack, 1)
                else:
                    e.wait_ge(s_pack, (g - 1) * NC + c + 1)
                    e.tensor_tensor(dst, dst, src, ALU.add).then_inc(s_pack, 1)

            def group(g):
                first = isinstance(g, int)
                for c in range(NC):
                    e.wait_ge(s_adj[c % NBUF], 16 * (NC // NBUF * g + c // NBUF + 1))
                    e.wait_ge(s_chk, g * NC + c + 1)
                    e.tensor_tensor(largest, largest, adj_sb[:, c % NBUF].rearrange("p t c -> p (t c)"),
                                    ALU.max).then_inc(s_chk, 1)
                    if c:
                        pack(g, c - 1)
                    if first and c % 2 == 0 and c < NC - 2:
                        split_rest(c // 2 + 1)
                    if not first:
                        if c == spot(5):
                            dve_v(e, fast, g - 1, g - 1, True, True)
                        if c == spot(8):
                            dve_x1(e, fast, g - 1)
                        if c == spot(13):
                            dve_h(e, fast, g - 1)
                        if c == spot(14):
                            dve_e(e, fast, g - 1)
                pack(g, NC - 1)
                e.wait_ge(s_mul, NP * (g + 1))
                dve_y(e, fast, g, g)

            split_rest(0)
            group(0)
            e.wait_ge(s_w, W_ALL)
            e.tensor_scalar(b_sq[:, :], onesq[:, :], b_col[:, :], None, ALU.mult).then_inc(s_bsq, 1)
            e.tensor_tensor(hsum, W_sb, W_sb, ALU.mult).then_inc(s_hbound, 1)
            e.wait_ge(s_hbound, 1)
            e.reduce_sum(wide[:, 0:1], hsum, AX).then_inc(s_hbound, 1)
            e.tensor_scalar(wide[:, 1:2], b_col[:, :], b_col[:, :], (4 / H_MAX) ** 2, ALU.mult, ALU.mult)
            e.wait_ge(s_hbound, 2)
            e.tensor_scalar(wide[:, 0:1], wide[:, 0:1], D * (4 / 3 / H_MAX) ** 2, None, ALU.mult)\
                .then_inc(s_hbound, 1)
            e.wait_ge(s_hbound, 3)
            e.tensor_tensor(top[:, 3:4], wide[:, 0:1], wide[:, 1:2], ALU.max).then_inc(s_hbound, 1)
            e.wait_ge(s_setup, 1)
            e.tensor_copy(WT[:, :], E0[:, 0:D])
            e.tensor_copy(u12[:, :], E0[:, D:D + 2])
            e.tensor_tensor(c12[:, :], E0[:, D + 2:D + 4], biases[:, 2 * D:2 * D + 2], ALU.add)\
                .then_inc(s_setc, 1)
            some(e, 1, G, group)
            e.wait_ge(s_chk, G * NC + 1)
            e.reduce_max(top[:, 0:1], largest, AX)
            dve_v(e, fast, G - 1, G - 1, True, True)
            dve_x1(e, fast, G - 1)
            dve_h(e, fast, G - 1)
            dve_e(e, fast, G - 1)

            e1, e2 = e12[:, 0, :], e12[:, 1, :]

            def tops_of_e2(n):
                e.tensor_scalar(lt, e2, -1.0, None, ALU.mult).then_inc(s_minus, 1)
                e.reduce_max(top[:, 1:2], e2, AX)
                e.wait_ge(s_minus, n)
                e.reduce_max(top[:, 2:3], lt, AX).then_inc(s_top, 1)

            def wide_flag(n):
                e.tensor_tensor(wide[:, 2:3], tops[:, 1:2], tops[:, 2:3], ALU.add).then_inc(s_span, 1)
                e.wait_ge(s_span, 2 * n - 1)
                e.scalar_tensor_tensor(wide[:, 3:4], wide[:, 2:3], 1 / SPAN, tops[:, 3:4], ALU.mult, ALU.max)\
                    .then_inc(s_span, 1)
                e.wait_ge(s_span, 2 * n)
                e.tensor_scalar(flag[:, 1:2], wide[:, 3:4], 1.0, None, ALU.is_gt).then_inc(s_wide, 1)

            e.wait_ge(s_hbound, 4)
            e.wait_ge(fast["e_copied"], G)
            tops_of_e2(1)
            e.wait_ge(fast["x1_stored"], 16 * G)
            e.wait_ge(s_all, 1)
            e.tensor_scalar(flag[:, 0:1], tops[:, 0:1], 2.0, None, ALU.is_ge).then_inc(s_flag, 1)
            wide_flag(1)
            e.wait_ge(s_flag, 1)
            with e.If(e.value_load(flag[0:1, 0:1], min_val=0, max_val=1) > 0):
                e.wait_ge(fast["e1_stored"], 16 * G)
                e.memset(edges[:, :, :].rearrange("p j r -> p (j r)").bitcast(I32), 0).then_inc(g_zero, 1)
                e.wait_ge(g_zero, 1)
                e.sem_inc(g_pack, 1)
                with e.Fori(0, G) as g:
                    for m, (compare, value, w) in enumerate(MASKS):
                        with e.Fori(0, NC) as c:
                            k = (g * NM + m) * NC + c
                            e.wait_ge(g_in, 16 * (k + 1))
                            flat = adj_sb[:, 0].rearrange("p t c -> p (t c)")
                            e.tensor_scalar(flat, flat, value, None, compare).then_inc(g_mask, 1)
                            if w is None:
                                e.wait_ge(g_evac, 2 * (k + 1) + 2)
                                dst = edges[:, ds(c * CB, CB), :].rearrange("p j r -> p (j r)")
                                e.tensor_tensor(dst, dst, adjT[:, 0:2, :].rearrange("p n c -> p (n c)"),
                                                ALU.add).then_inc(g_pack, 1)
                        if w is not None:
                            n = g * (NM - 1) + m
                            e.wait_ge(g_mul, (n + 1) * NC)
                            dve_y(e, general, n, g)
                            dve_v(e, general, n, g, m == 0, m == NM - 2)
                    dve_x1(e, general, g)
                    dve_h(e, general, g)
                    dve_e(e, general, g)
                e.wait_ge(general["x1_stored"], 16 * G)
                e.wait_ge(general["e1_stored"], 16 * G)
                e.wait_ge(g_pack, G * NC + 1)
                e.wait_ge(general["e_copied"], G)
                tops_of_e2(2)
                e.wait_ge(s_all, 2)
                wide_flag(2)
                e.wait_ge(s_wide, 2)

            links = [0]

            def link(ins):
                links[0] += 1
                ins.then_inc(s_mid, 1)
                e.wait_ge(s_mid, links[0])

            e.wait_ge(s_wide, 1)
            with e.If(e.value_load(flag[0:1, 1:2], min_val=0, max_val=1) > 0):
                e.tensor_copy(tt, e1)
                e.tensor_copy(lt, e2).then_inc(wd["e2_turned"], 1)
                m, nm, den, rden, w_var, w_sd, w_rs = [tile_col[:, n:n + 1] for n in range(7)]
                e.wait_ge(wd["e2_stored"], 16)
                with e.Fori(0, JB) as i:
                    e.wait_ge(wd["adj_in"], 16 * (i + 1))
                    e.tensor_scalar(adj_row, adj_row, 0.0, NO_EDGE, ALU.is_le, ALU.mult).then_inc(wd["penalty"], 1)
                    e.wait_ge(wd["score"], i + 1)
                    e.scalar_tensor_tensor(score, score, SLOPE, score, ALU.mult, ALU.max)\
                        .then_inc(wd["leaky"], 1)
                    e.wait_ge(wd["penalty"], i + 1)
                    e.wait_ge(wd["leaky"], i + 1)
                    e.tensor_tensor(score, score, adj_row, ALU.add).then_inc(wd["masked"], 1)
                    e.wait_ge(wd["masked"], i + 1)
                    e.reduce_max(m, score, AX).then_inc(wd["max"], 1)
                    e.wait_ge(wd["max"], i + 1)
                    e.tensor_scalar(nm, m, -1.0, None, ALU.mult).then_inc(wd["max_negated"], 1)
                    e.wait_ge(wd["exp"], i + 1)
                    e.reduce_sum(den, score, AX).then_inc(wd["sum"], 1)
                    e.wait_ge(wd["sum"], i + 1)
                    e.reciprocal(rden, den).then_inc(wd["scale"], 1)
                    e.wait_ge(wd["scale"], 2 * i + 1)
                    e.wait_ge(wd["x1_in"], 16 * (i + 1))
                    e.wait_ge(wd["product"], NC * (i + 1))
                    e.scalar_tensor_tensor(v_tile, E1[:, 0:D], rden, x1_tile, ALU.mult, ALU.add).then_inc(wd["v"], 1)
                    e.wait_ge(wd["v"], i + 1)
                    e.bn_stats(stats[:, 0, :], v_tile).then_inc(wd["stats"], 1)
                    e.wait_ge(wd["stats"], i + 1)
                    e.memset(w_var, 0.0)
                    e.bn_aggr(mv[:, 0, :], stats[:, 0, :]).then_inc(wd["mean"], 1)
                    e.wait_ge(wd["mean"], i + 1)
                    e.tensor_scalar(w_var, mv[:, 0, 1:2], EPS, None, ALU.add).then_inc(wd["var"], 1)
                    e.wait_ge(wd["sd"], i + 1)
                    e.reciprocal(w_rs, w_sd).then_inc(wd["scale"], 1)
                    e.wait_ge(wd["scale"], 2 * i + 2)
                    e.tensor_scalar(out_tile, v_tile, mv[:, 0, 0:1], w_rs, ALU.subtract, ALU.mult)\
                        .then_inc(wd["out"], 1)
                    e.wait_ge(wd["stored"], 16 * (i + 2))
            with e.If(e.value_load(flag[0:1, 1:2], min_val=0, max_val=1) < 1):
                e.tensor_scalar(ne[:, 0:1], tops[:, 1:2], -1.0, None, ALU.mult)
                e.tensor_scalar(ne[:, 1:2], tops[:, 1:2], -SLOPE, None, ALU.mult).then_inc(s_exps, 1)
                e.tensor_scalar(e2s, e2, STEEP, None, ALU.mult).then_inc(s_exps, 1)
                link(e.tensor_scalar(tt, e1, tops[:, 1:2], None, ALU.add))
                link(e.tensor_scalar(lt, tt, SLOPE, None, ALU.mult))
                link(e.tensor_tensor(mx, tt, lt, ALU.max))
                e.tensor_tensor(ta, tt, mx, ALU.subtract)
                e.tensor_tensor(tc, lt, mx, ALU.subtract).then_inc(s_exps, 1)
                e.wait_ge(s_exps, 3)
                for k, (f, full_scale) in enumerate(((bb, BSC * LO), (dd, LO))):
                    e.wait_ge(s_exp, k + 1)
                    e.tensor_scalar(factor[k], f, full_scale, None, ALU.mult).then_inc(s_factor, 1)
                for k in range(2):
                    e.wait_ge(s_factor, k + 1)
                    one = tab[:, k, :, D]
                    link(e.tensor_scalar(one, factor[k], 1.0 / LO, None, ALU.mult))
                    e.scalar_tensor_tensor(tab[:, k, :, TB + D], one, -LO, factor[k], ALU.mult, ALU.add)
                e.wait_ge(s_exp, 3)
                e.tensor_scalar(a_row, a_row, 1.0 / BSC, None, ALU.mult).then_inc(s_factor, 1)

                def low(q):
                    v, k = divmod(q, 2)
                    sl = slice(v * VB, (v + 1) * VB)
                    e.wait_ge(s_high, q + 1)
                    e.scalar_tensor_tensor(tab[:, k, sl, TB:TB + D], tab[:, k, sl, 0:D], -LO, stage[:, k],
                                           ALU.mult, ALU.add).then_inc(s_low, 1)

                def edge_bits(g, c, u):
                    e.tensor_scalar(u, edges[:, c * CB:(c + 1) * CB, :].rearrange("p j r -> p (j r)"),
                                    bits[:, ds(g, 1)], None, ALU.bitwise_and).then_inc(s_bit, 1)

                def pos_mask(g, c, u):
                    k = g * NC + c
                    e.wait_ge(s_bit, k + 1)
                    e.wait_ge(s_gate, k + 1)
                    ge(e, s_used, k - 1)
                    e.tensor_tensor(pos[:, c % 2], u, gate[:, c % 2], ALU.min).then_inc(s_pos, 1)

                def neg_mask(g, c, u):
                    k = g * NC + c
                    e.wait_ge(s_pos, k + 1)
                    e.tensor_tensor(neg[:, c % 2], u, pos[:, c % 2], ALU.subtract).then_inc(s_neg, 1)

                def neg_parts(g):
                    e.wait_ge(s_hsc, 1)
                    for t in range(GT):
                        sums_done(e, g, t)
                        e.tensor_scalar(neg_part[:, t, :], ps[:, GT + t, 0:2 * TB], c_row[:, ds(g * GT + t, 1)],
                                        None, ALU.mult).then_inc(s_npart, 1)

                def add_low(g):
                    e.wait_ge(s_add, g + 1)
                    e.scalar_tensor_tensor(num_den, pos_part[:, :, TB:2 * TB], 1.0 / LO,
                                           pos_part[:, :, 0:TB], ALU.mult, ALU.add).then_inc(s_num, 1)

                def fill_empty(g):
                    num, den = num_den[:, :, 0:D], num_den[:, :, D]
                    e.wait_ge(s_num, g + 1)
                    e.tensor_scalar(zr[:, :], den, 0.0, None, ALU.is_equal).then_inc(s_zr, 1)
                    e.wait_ge(s_zr, g + 1)
                    e.scalar_tensor_tensor(dn[:, :], zr[:, :], float(N), den, ALU.mult, ALU.add)
                    for t in range(GT):
                        last = e.scalar_tensor_tensor(num[:, t, :], hsum[:, :], zr[:, t:t + 1], num[:, t, :],
                                                      ALU.mult, ALU.add)
                    last.then_inc(s_dn, 1)

                def add_x1(g):
                    e.wait_ge(s_dn, g + 1)
                    e.reciprocal(rd[:, :], dn[:, :]).then_inc(s_rd, 1)
                    e.wait_ge(s_x1in, 16 * (g + 1))
                    e.wait_ge(s_rd, g + 1)
                    for t in range(GT):
                        last = e.scalar_tensor_tensor(v2[:, t, :], num_den[:, t, 0:D], rd[:, t:t + 1],
                                                      x1_in[:, t, :], ALU.mult, ALU.add)
                    last.then_inc(s_v2, 1)

                def statistics(g):
                    e.wait_ge(s_v2, g + 1)
                    for t in range(GT):
                        last = e.bn_stats(stats[:, t, :], v2[:, t, :])
                    last.then_inc(s_st2, 1)

                def variance(g):
                    e.wait_ge(s_st2, g + 1)
                    e.memset(var[:, :], 0.0)
                    for t in range(GT):
                        last = e.bn_aggr(mv[:, t, :], stats[:, t, :])
                    last.then_inc(s_mv2, 1)
                    e.wait_ge(s_mv2, g + 1)
                    e.tensor_scalar(var[:, :], mv[:, :, 1], EPS, None, ALU.add).then_inc(s_var2, 1)

                def scale_down(g):
                    e.wait_ge(s_sd2, g + 1)
                    e.reciprocal(rs[:, :], sd[:, :]).then_inc(s_rs2, 1)
                    e.wait_ge(s_rs2, g + 1)
                    for t in range(GT):
                        last = e.tensor_scalar(out_sb[:, t, :], v2[:, t, :], mv[:, t, 0:1], rs[:, t:t + 1],
                                               ALU.subtract, ALU.mult)
                    last.then_inc(s_out, 1)

                STEPS = [(0, neg_parts), (3, add_low), (5, fill_empty), (7, add_x1), (9, statistics),
                         (10, variance), (13, scale_down)]

                def group1(g):
                    known = isinstance(g, int)
                    if not known:
                        e.wait_ge(s_neg, g * NC)
                        edge_bits(g, 0, bit_buf[:, 0])
                    for c in range(NC):
                        if known and g == 0 and c % 2:
                            low(c - 1)
                            low(c)
                        if known:
                            u = neg[:, c % 2].bitcast(U16)
                            ge(e, s_used, g * NC + c - 1)
                            edge_bits(g, c, u)
                            pos_mask(g, c, u)
                            neg_mask(g, c, u)
                        else:
                            pos_mask(g, c, bit_buf[:, c % 2])
                            if c + 1 < NC:
                                e.wait_ge(s_neg, g * NC + c)
                                edge_bits(g, c + 1, bit_buf[:, (c + 1) % 2])
                            neg_mask(g, c, bit_buf[:, c % 2])
                        if known and g == 1 and c == 0:
                            e.wait_ge(s_hs, 1)
                            e.tensor_copy(hsum[:, :], h_all).then_inc(s_hsc, 1)
                        for k, step in STEPS:
                            if not (known and g == 0) and c == spot(k):
                                step(g - 1)

                group1(0)
                group1(1)
                some(e, 2, G, group1)
                for _, step in STEPS:
                    step(G - 1)

        @blk.scalar
        def _(e):
            def double(S, g):
                if isinstance(g, int) and g == 0:
                    e.activation(scale[:, :], pow2[:, 0, 0:1], ACT.Copy).then_inc(S["scale_ready"], 1)
                    e.wait_ge(S["scale_ready"], 1)
                else:
                    e.activation(scale[:, :], scale[:, :], ACT.Copy, scale=2.0).then_inc(S["scale_ready"], 1)
                    e.wait_ge(S["scale_ready"], g + 1)

            e.wait_ge(s_const, 1)
            double(fast, 0)

            def split_high(v):
                sl = slice(v * VB, (v + 1) * VB)
                e.wait_ge(s_x, 16 * (v + 1))
                e.activation(v_hl[:, sl, 0:D], x_in[:, sl, :], ACT.Copy).then_inc(s_vh, 1)

            def split_low(v):
                sl = slice(v * VB, (v + 1) * VB)
                e.wait_ge(s_vr, v + 1)
                e.activation(v_hl[:, sl, D:2 * D], x_in[:, sl, :], ACT.Copy, scale=LO).then_inc(s_vl, 1)

            def group(g):
                first = isinstance(g, int)
                if not first:
                    double(fast, g)
                for c in range(NC):
                    for i in range(2):
                        q = g * NP + 2 * c + i
                        slot = (2 * c + i) % 4
                        e.wait_ge(s_turn, q + 1)
                        ge(e, s_mul, q - 3)
                        ge(e, s_pack, g * NC + c - 1)
                        e.activation(adjT[:, slot, :], turned(i), ACT.Relu,
                                     scale=scale[:, :]).then_inc(s_evac, 1)
                    if first and c < NC - 2:
                        (split_low if c % 2 else split_high)(c // 2 + 1)
                    if not first:
                        if c == spot(6):
                            act_sd(e, fast, g - 1)
                        if c == spot(10):
                            act_x1T(e, fast, g - 1)

            split_high(0)
            split_low(0)
            group(0)
            e.wait_ge(s_setc, 1)
            some(e, 1, G, group)
            act_sd(e, fast, G - 1)
            act_x1T(e, fast, G - 1)

            e.wait_ge(s_flag, 1)
            with e.If(e.value_load(flag[0:1, 0:1], min_val=0, max_val=1) > 0):
                double(general, 0)
                e.sem_inc(g_evac, 2)
                with e.Fori(0, G) as g:
                    for m, (_, _, w) in enumerate(MASKS):
                        with e.Fori(0, NC) as c:
                            k = (g * NM + m) * NC + c
                            for i in range(2):
                                e.wait_ge(g_turn, 2 * k + i + 3)
                                if w is None:
                                    e.wait_ge(g_pack, g * NC + c + 1)
                                e.activation(adjT[:, i, :], turned(i), ACT.Copy,
                                             scale=scale[:, :]).then_inc(g_evac, 1)
                    act_sd(e, general, g)
                    act_x1T(e, general, g)
                    double(general, g + 1)
                e.wait_ge(s_wide, 2)

            e.wait_ge(s_wide, 1)
            with e.If(e.value_load(flag[0:1, 1:2], min_val=0, max_val=1) > 0):
                nm, w_var, w_sd = [tile_col[:, n:n + 1] for n in (1, 4, 5)]
                e.wait_ge(wd["e2_turned"], 2)
                e.activation(e2_T, E0[0:JB, 0:P], ACT.Copy).then_inc(wd["e2_copied"], 1)
                e.wait_ge(wd["e2_row_in"], 16)
                with e.Fori(0, JB) as i:
                    e.wait_ge(wd["stored"], 16 * (i + 1))
                    e.activation(score, e2_row, ACT.Identity, bias=tt[:, ds(i, 1)]).then_inc(wd["score"], 1)
                    e.wait_ge(wd["max_negated"], i + 1)
                    e.activation(score, score, ACT.Exp, bias=nm).then_inc(wd["exp"], 1)
                    with e.Fori(0, NC) as c:
                        e.wait_ge(wd["turned"], i * NC + c + 1)
                        e.activation(prob_T, E0t, ACT.Copy).then_inc(wd["copied"], 1)
                    e.wait_ge(wd["var"], i + 1)
                    e.activation(w_sd, w_var, ACT.Sqrt).then_inc(wd["sd"], 1)
            with e.If(e.value_load(flag[0:1, 1:2], min_val=0, max_val=1) < 1):
                e.wait_ge(s_exps, 1)
                e.activation(bb, e12[:, 1, :], ACT.Exp, bias=ne[:, 0:1]).then_inc(s_exp, 1)
                e.activation(dd, e12[:, 1, :], ACT.Exp, bias=ne[:, 1:2], scale=SLOPE).then_inc(s_exp, 1)
                e.wait_ge(s_exps, 3)
                e.activation(a_row, ta, ACT.Exp)
                e.activation(c_row, tc, ACT.Exp).then_inc(s_exp, 1)

                def high(q):
                    v, k = divmod(q, 2)
                    e.wait_ge(s_full, q + 1)
                    e.activation(tab[:, k, v * VB:(v + 1) * VB, 0:D], stage[:, k], ACT.Copy, scale=1.0 / LO)\
                        .then_inc(s_high, 1)

                def chunk(g, c, n, turn):
                    ge(e, s_pos, g * NC + c - 1)
                    for jj in range(CB):
                        j = c * CB + jj
                        last = e.activation(gate[:, n, jj * GR:(jj + 1) * GR].rearrange("p (t c) -> p t c", t=GT),
                                            e1_row[:, turn, :].rearrange("p (c t) -> p t c", t=GT), ACT.Relu,
                                            bias=e2s[:, j:j + 1], scale=STEEP)
                    last.then_inc(s_gate, 1)

                def pos_parts(g):
                    e.wait_ge(s_factor, 3)
                    e.wait_ge(s_low, NQ)
                    e.wait_ge(s_hsc, 1)
                    for t in range(GT):
                        sums_done(e, g, t)
                        e.activation(pos_part[:, t, :], ps[:, t, 0:2 * TB], ACT.Copy,
                                     scale=a_row[:, ds(g * GT + t, 1)]).then_inc(s_ppart, 1)

                def act_sd2(g):
                    e.wait_ge(s_var2, g + 1)
                    e.activation(sd[:, :], var[:, :], ACT.Sqrt).then_inc(s_sd2, 1)

                def group1(g, turn, last=False):
                    e.wait_ge(s_row[turn], 8 * (g - turn) + 16)
                    for c in range(NC):
                        if isinstance(g, int) and g == 0 and c % 2:
                            high(c - 1)
                            high(c)
                        chunk(g, c, c % 2, turn)
                        if not (isinstance(g, int) and g == 0):
                            if c == spot(1):
                                pos_parts(g - 1)
                            if c == spot(11):
                                act_sd2(g - 1)

                group1(0, 0)
                in_twos(e, G, group1)
                pos_parts(G - 1)
                act_sd2(G - 1)

        @blk.tensor
        def _(e):
            e.wait_ge(s_ident, 4)

            def group(g):
                first = isinstance(g, int)
                for i in range(NP + 2):
                    if i < NP:
                        c = i // 2
                        if i % 2 == 0:
                            e.wait_ge(s_adj[c % NBUF], 16 * (NC // NBUF * g + c // NBUF + 1))
                        ge(e, s_evac, g * NP + i - 1)
                        turn(e, c % NBUF, i % 2, i % 2).then_inc(s_turn, 1)
                    if i >= 2:
                        q = i - 2
                        if first and q % 4 == 0:
                            e.wait_ge(s_vl, q // 4 + 1)
                        if q == 0 and not first:
                            e.wait_ge(fast["y_ready"], g)
                        if i >= NP:
                            e.wait_ge(s_evac, g * NP + q + 1)
                        multiply(e, q % 4, 2 * q, q == 0, q == NP - 1).then_inc(s_mul, 1)
                        if not first and q % 2:
                            c = q // 2
                            if c == spot(3):
                                pe_o(e, fast, g - 1, w_sb[0], True)
                            if c == spot(9):
                                pe_x1T(e, fast, g - 1)
                            if c == spot(11):
                                pe_h(e, fast, g - 1)

            group(0)
            e.wait_ge(s_w, W_ALL)
            e.transpose(E0[:, 0:D], W_sb[:, :], idf[:, :])
            e.matmul(E0[:, D:D + 2], W_sb[:, :], we[:, :], start=True, stop=True)
            e.wait_ge(s_bsq, 1)
            e.matmul(E0[:, D + 2:D + 4], b_sq[:, :], we[:, :], start=True, stop=True).then_inc(s_setup, 1)
            e.wait_ge(s_setc, 1)
            some(e, 1, G, group)
            pe_o(e, fast, G - 1, w_sb[0], True)
            pe_x1T(e, fast, G - 1)
            pe_h(e, fast, G - 1)

            e.wait_ge(s_flag, 1)
            with e.If(e.value_load(flag[0:1, 0:1], min_val=0, max_val=1) > 0):
                e.sem_inc(g_turn, 2)
                with e.Fori(0, G) as g:
                    for m, (_, _, w) in enumerate(MASKS):
                        n = g * (NM - 1) + m

                        def chunk(c, start, stop):
                            k = (g * NM + m) * NC + c
                            e.wait_ge(g_mask, k + 1)
                            e.wait_ge(g_evac, 2 * k + 2)
                            for i in range(2):
                                turn(e, 0, i, i).then_inc(g_turn, 1)
                            for i in range(2):
                                if w is not None:
                                    e.wait_ge(g_evac, 2 * k + i + 3)
                                    last = multiply(e, i, c * CB + 2 * i, start and i == 0, stop and i == 1)
                            if w is not None:
                                last.then_inc(g_mul, 1)

                        chunk(0, True, False)
                        some(e, 1, NC - 1, lambda c: chunk(c, False, False))
                        chunk(NC - 1, False, True)
                        if w is not None:
                            pe_o(e, general, n, w, m == 0)
                    pe_x1T(e, general, g)
                    pe_h(e, general, g)
                e.wait_ge(s_wide, 2)

            e.wait_ge(s_wide, 1)
            with e.If(e.value_load(flag[0:1, 1:2], min_val=0, max_val=1) > 0):
                e.wait_ge(wd["e2_turned"], 1)
                e.transpose(E0[0:JB, 0:P], lt, idf).then_inc(wd["e2_turned"], 1)
                e.wait_ge(wd["e2_copied"], 1)
                e.sem_inc(wd["copied"], 1)
                with e.Fori(0, JB) as i:
                    e.wait_ge(wd["exp"], i + 1)

                    for c in range(NC):
                        k = i * NC + c
                        e.wait_ge(wd["copied"], k + 1)
                        for jj in range(CB):
                            last = e.transpose(E0t[:, jj, :], score[:, c * CC + jj * P:c * CC + (jj + 1) * P], idf)
                        last.then_inc(wd["turned"], 1)
                        e.wait_ge(wd["copied"], k + 2)
                        for jj in range(CB):
                            last = e.matmul(E1[:, 0:D], prob_T[:, jj, :],
                                            h_sb[:, c * CB + jj, :],
                                            start=c + jj == 0, stop=c * CB + jj == JB - 1)
                        last.then_inc(wd["product"], 1)
            with e.If(e.value_load(flag[0:1, 1:2], min_val=0, max_val=1) < 1):
                def pair(g, c2, start=False, stop=False):
                    for n in range(2):
                        c = 2 * c2 + n
                        e.wait_ge(s_neg, g * NC + c + 1)
                        if isinstance(g, int):
                            e.wait_ge(s_low, 2 * (c2 + 1))
                        for t in range(GT):
                            if start and n == 0:
                                ge(e, s_ppart, GT * (g - 1) + t + 1)
                                ge(e, s_npart, GT * (g - 1) + t + 1)
                                if t == GT - 1 and not isinstance(g, int):
                                    e.wait_ge(s_hsc, 1)
                            for jj in range(CB):
                                lhs = slice(jj * GR + t * P, jj * GR + (t + 1) * P)
                                for k, mask in enumerate((pos, neg)):
                                    last = e.matmul(ps[:, t + GT * k, 0:2 * TB], mask[:, n, lhs],
                                                    tab[:, k, ds(c * CB + jj, 1), :].rearrange("p a c -> p (a c)"),
                                                    start=start and n == 0 and jj == 0,
                                                    stop=stop and n == 1 and jj == CB - 1)
                            if stop and n == 1 and t < GT - 1:
                                last.then_inc(s_acc, 1)
                        last.then_inc(s_used, 1)
                        if isinstance(g, int):
                            for j in range(c * CB, (c + 1) * CB):
                                last = e.matmul(h_all, onesq[:, :], h_sb[:, j, :], start=False, stop=j == JB - 1,
                                                skip_group_check=True)
                            if c == NC - 1:
                                last.then_inc(s_hs, 1)

                def group1(g):
                    for c2 in range(PAIRS):
                        pair(g, c2, start=c2 == 0, stop=c2 == PAIRS - 1)

                group1(0)
                some(e, 1, G, group1)


_INS = ["x", "adj", "L0_gnn_w1", "L0_gnn_w2", "L0_gnn_w3", "L0_gnn_bias", "L1_gnn_W", "L1_gnn_b",
        "L1_gnn_we1", "L1_gnn_be1", "L1_gnn_we2", "L1_gnn_be2"]


def kernel(**inputs):
    import numpy as np
    import concourse.bacc as bacc
    from concourse.bass_utils import run_bass_kernel_spmd as run

    nc = bacc.Bacc("TRN2", target_bir_lowering=False, num_devices=1)
    arrays, args = {}, []
    for name in _INS:
        a = np.ascontiguousarray(inputs[name])
        arrays[name] = a
        args.append(nc.dram_tensor(name, a.shape, mybir.dt.from_np(a.dtype), kind="ExternalInput").ap())
    out = nc.dram_tensor("out", inputs["x"].shape, F32, kind="ExternalOutput").ap()
    build(nc, *args, out)
    return run(nc, [arrays], core_ids=[0]).results[0]["out"]
```
